# Optimizing a Trainium2 kernel written in Bass

```python
import numpy as np
import jax
import jax.numpy as jnp

def _softmax(x, axis=-1):
    return jax.nn.softmax(x, axis=axis)

def _gelu(x):
    return jax.nn.gelu(x, approximate=True)

def _silu(x):
    return jax.nn.silu(x)

def _sigmoid(x):
    return jax.nn.sigmoid(x)

def _layernorm(x, axis=-1, eps=1e-05):
    m = jnp.mean(x, axis=axis, keepdims=True)
    v = jnp.var(x, axis=axis, keepdims=True)
    return (x - m) / jnp.sqrt(v + eps)

def _scatter_add(tgt, idx, src, axis=0):
    return tgt.at[idx].add(src)

def _segment_sum(src, seg, n):
    return jax.ops.segment_sum(src, seg, n)
kernel_name = 'mk_dlrm_tower_d1_rec_r8_812003'

def setup_inputs(seed: int=0):
    np.random.seed(seed)
    _w = jnp.asarray

    def _rec_inputs():
        import jax
        import jax.numpy as jnp
        _tk = jax.random.key(seed)
        ids = jnp.stack([jax.random.randint(jax.random.fold_in(_tk, 200 + f), (512,), 0, v, jnp.int32) for f, v in enumerate([1000, 1000, 12500, 125000, 1000, 1250, 12500, 1000, 12500, 12500, 1250, 12500, 1000, 1250, 1250, 1000, 1000, 12500, 12500, 1250, 1250, 12500, 1250, 1000, 1000, 1250])], axis=1)
        tbl_0 = 0.05 * jax.random.normal(jax.random.fold_in(_tk, 500 + 0), (1000, 128), jnp.float32)
        tbl_1 = 0.05 * jax.random.normal(jax.random.fold_in(_tk, 500 + 1), (1000, 128), jnp.float32)
        tbl_2 = 0.05 * jax.random.normal(jax.random.fold_in(_tk, 500 + 2), (12500, 128), jnp.float32)
        tbl_3 = 0.05 * jax.random.normal(jax.random.fold_in(_tk, 500 + 3), (125000, 128), jnp.float32)
        tbl_4 = 0.05 * jax.random.normal(jax.random.fold_in(_tk, 500 + 4), (1000, 128), jnp.float32)
        tbl_5 = 0.05 * jax.random.normal(jax.random.fold_in(_tk, 500 + 5), (1250, 128), jnp.float32)
        tbl_6 = 0.05 * jax.random.normal(jax.random.fold_in(_tk, 500 + 6), (12500, 128), jnp.float32)
        tbl_7 = 0.05 * jax.random.normal(jax.random.fold_in(_tk, 500 + 7), (1000, 128), jnp.float32)
        tbl_8 = 0.05 * jax.random.normal(jax.random.fold_in(_tk, 500 + 8), (12500, 128), jnp.float32)
        tbl_9 = 0.05 * jax.random.normal(jax.random.fold_in(_tk, 500 + 9), (12500, 128), jnp.float32)
        tbl_10 = 0.05 * jax.random.normal(jax.random.fold_in(_tk, 500 + 10), (1250, 128), jnp.float32)
        tbl_11 = 0.05 * jax.random.normal(jax.random.fold_in(_tk, 500 + 11), (12500, 128), jnp.float32)
        tbl_12 = 0.05 * jax.random.normal(jax.random.fold_in(_tk, 500 + 12), (1000, 128), jnp.float32)
        tbl_13 = 0.05 * jax.random.normal(jax.random.fold_in(_tk, 500 + 13), (1250, 128), jnp.float32)
        tbl_14 = 0.05 * jax.random.normal(jax.random.fold_in(_tk, 500 + 14), (1250, 128), jnp.float32)
        tbl_15 = 0.05 * jax.random.normal(jax.random.fold_in(_tk, 500 + 15), (1000, 128), jnp.float32)
        tbl_16 = 0.05 * jax.random.normal(jax.random.fold_in(_tk, 500 + 16), (1000, 128), jnp.float32)
        tbl_17 = 0.05 * jax.random.normal(jax.random.fold_in(_tk, 500 + 17), (12500, 128), jnp.float32)
        tbl_18 = 0.05 * jax.random.normal(jax.random.fold_in(_tk, 500 + 18), (12500, 128), jnp.float32)
        tbl_19 = 0.05 * jax.random.normal(jax.random.fold_in(_tk, 500 + 19), (1250, 128), jnp.float32)
        tbl_20 = 0.05 * jax.random.normal(jax.random.fold_in(_tk, 500 + 20), (1250, 128), jnp.float32)
        tbl_21 = 0.05 * jax.random.normal(jax.random.fold_in(_tk, 500 + 21), (12500, 128), jnp.float32)
        tbl_22 = 0.05 * jax.random.normal(jax.random.fold_in(_tk, 500 + 22), (1250, 128), jnp.float32)
        tbl_23 = 0.05 * jax.random.normal(jax.random.fold_in(_tk, 500 + 23), (1000, 128), jnp.float32)
        tbl_24 = 0.05 * jax.random.normal(jax.random.fold_in(_tk, 500 + 24), (1000, 128), jnp.float32)
        tbl_25 = 0.05 * jax.random.normal(jax.random.fold_in(_tk, 500 + 25), (1250, 128), jnp.float32)
        _rk = jax.random.fold_in(_tk, 7)
        r_dense_features = 7.22013e-05 + 1.00017 * jax.random.normal(jax.random.fold_in(_rk, 101), (512, 128), jnp.float32)
        W_top1 = 0.0456912 * jax.random.normal(jax.random.fold_in(_tk, 801), (479, 512), jnp.float32)
        W_top2 = 0.0441942 * jax.random.normal(jax.random.fold_in(_tk, 802), (512, 256), jnp.float32)
        W_top3 = 0.0625 * jax.random.normal(jax.random.fold_in(_tk, 803), (256, 1), jnp.float32)
        b_top1 = jnp.zeros((512,), jnp.float32)
        b_top2 = jnp.zeros((256,), jnp.float32)
        return (r_dense_features, ids, tbl_0, tbl_1, tbl_2, tbl_3, tbl_4, tbl_5, tbl_6, tbl_7, tbl_8, tbl_9, tbl_10, tbl_11, tbl_12, tbl_13, tbl_14, tbl_15, tbl_16, tbl_17, tbl_18, tbl_19, tbl_20, tbl_21, tbl_22, tbl_23, tbl_24, tbl_25, W_top1, b_top1, W_top2, b_top2, W_top3)
    r_dense_features, ids, tbl_0, tbl_1, tbl_2, tbl_3, tbl_4, tbl_5, tbl_6, tbl_7, tbl_8, tbl_9, tbl_10, tbl_11, tbl_12, tbl_13, tbl_14, tbl_15, tbl_16, tbl_17, tbl_18, tbl_19, tbl_20, tbl_21, tbl_22, tbl_23, tbl_24, tbl_25, W_top1, b_top1, W_top2, b_top2, W_top3 = _rec_inputs()

    def _L0_rec_setup():
        import jax, jax.numpy as jnp
        import numpy as np
        FEATURE_NUM = 27
        key = jax.random.key(seed)
        k1, k2 = jax.random.split(key)
        B, N, D = (8192, FEATURE_NUM - 1, 128)
        dense_features = jax.random.normal(k1, (B, D), dtype=jnp.float32)
        sparse_features = jax.random.normal(k2, (B, N, D), dtype=jnp.float32)
        return {'dense_features': dense_features, 'sparse_features': sparse_features}
    _L0_rec_all = _L0_rec_setup()
    _L0_rec_in = {k: v for k, v in _L0_rec_all.items() if k in ()}
    del _L0_rec_all
    return {'r_dense_features': r_dense_features, 'ids': ids, 'tbl_0': tbl_0, 'tbl_1': tbl_1, 'tbl_2': tbl_2, 'tbl_3': tbl_3, 'tbl_4': tbl_4, 'tbl_5': tbl_5, 'tbl_6': tbl_6, 'tbl_7': tbl_7, 'tbl_8': tbl_8, 'tbl_9': tbl_9, 'tbl_10': tbl_10, 'tbl_11': tbl_11, 'tbl_12': tbl_12, 'tbl_13': tbl_13, 'tbl_14': tbl_14, 'tbl_15': tbl_15, 'tbl_16': tbl_16, 'tbl_17': tbl_17, 'tbl_18': tbl_18, 'tbl_19': tbl_19, 'tbl_20': tbl_20, 'tbl_21': tbl_21, 'tbl_22': tbl_22, 'tbl_23': tbl_23, 'tbl_24': tbl_24, 'tbl_25': tbl_25, 'W_top1': W_top1, 'b_top1': b_top1, 'W_top2': W_top2, 'b_top2': b_top2, 'W_top3': W_top3}

def reference(r_dense_features, ids, tbl_0, tbl_1, tbl_2, tbl_3, tbl_4, tbl_5, tbl_6, tbl_7, tbl_8, tbl_9, tbl_10, tbl_11, tbl_12, tbl_13, tbl_14, tbl_15, tbl_16, tbl_17, tbl_18, tbl_19, tbl_20, tbl_21, tbl_22, tbl_23, tbl_24, tbl_25, W_top1, b_top1, W_top2, b_top2, W_top3):
    import jax
    import jax.numpy as jnp

    def _L0_rec_ref(dense_features, sparse_features):
        import jax, jax.numpy as jnp
        import numpy as np
        FEATURE_NUM = 27
        combined = jnp.concatenate([dense_features[:, None, :], sparse_features], axis=1)
        interactions = jnp.einsum('bfd,bgd->bfg', combined, combined)
        iu, ju = jnp.triu_indices(FEATURE_NUM, k=1)
        return interactions[:, iu, ju]
    e = jnp.stack([tbl_0[ids[:, 0]], tbl_1[ids[:, 1]], tbl_2[ids[:, 2]], tbl_3[ids[:, 3]], tbl_4[ids[:, 4]], tbl_5[ids[:, 5]], tbl_6[ids[:, 6]], tbl_7[ids[:, 7]], tbl_8[ids[:, 8]], tbl_9[ids[:, 9]], tbl_10[ids[:, 10]], tbl_11[ids[:, 11]], tbl_12[ids[:, 12]], tbl_13[ids[:, 13]], tbl_14[ids[:, 14]], tbl_15[ids[:, 15]], tbl_16[ids[:, 16]], tbl_17[ids[:, 17]], tbl_18[ids[:, 18]], tbl_19[ids[:, 19]], tbl_20[ids[:, 20]], tbl_21[ids[:, 21]], tbl_22[ids[:, 22]], tbl_23[ids[:, 23]], tbl_24[ids[:, 24]], tbl_25[ids[:, 25]]], axis=1)
    z = _L0_rec_ref(r_dense_features, e)
    z = z.reshape(z.shape[0], -1)
    h = jnp.concatenate([z, r_dense_features], axis=1)
    h = jnp.maximum(h @ W_top1 + b_top1, 0.0)
    h = jnp.maximum(h @ W_top2 + b_top2, 0.0)
    y = h @ W_top3
    return y

_drawn_inputs = setup_inputs


def setup_inputs(seed=0):
    import zlib

    import numpy as np

    out = dict(_drawn_inputs(seed))
    spreads = {'b_top1': (0.0, 0.1), 'b_top2': (0.0, 0.1)}
    factors = {}
    for name, (base, spread) in spreads.items():
        noise = np.random.default_rng([zlib.crc32(name.encode()), seed]).standard_normal(out[name].shape)
        drawn = base * np.exp(spread * noise) if base else spread * noise
        out[name] = jnp.asarray(drawn.astype(out[name].dtype))
    for name, factor in factors.items():
        out[name] = (out[name] * factor).astype(out[name].dtype)
    return out
```

```python
import concourse.bass as bass
from concourse import mybir
from contextlib import ExitStack

P = 128
D = 128
TILES = 4
NF = 27
SLOTS = (NF - 1) // 2
NPAIR = NF * SLOTS
ZC = 3
ZP = NPAIR // ZC
H1, H2 = 512, 256
N1, N2 = H1 // P, H2 // P
QUADS = 4
QG = P // QUADS
HALVES = 2
GH = QG // HALVES
TR = 125
ROWS = [1000, 1000, 12500, 125000, 1000, 1250, 12500, 1000, 12500, 12500, 1250, 12500, 1000, 1250,
        1250, 1000, 1000, 12500, 12500, 1250, 1250, 12500, 1250, 1000, 1000, 1250]
N_ONEHOT = 10
ONEHOT = sorted(range(len(ROWS)), key=lambda f: ROWS[f])[:N_ONEHOT]
GATHERED = [f for f in range(len(ROWS)) if f not in ONEHOT]
ORDER = [0] + [1 + f for f in ONEHOT + GATHERED]
GRP = 4
GROUPS = [GATHERED[i:i + GRP] for i in range(0, len(GATHERED), GRP)]
KMAX = 10
KH = KMAX // 2
RING = 2
OHB = 3

C_ID = 0
C_ROW8 = C_ID + P
C_ROW10 = C_ROW8 + 8
C_FAR = C_ROW10 + 10
C_LAST = C_FAR + SLOTS
C_END = C_LAST + SLOTS


def partner(k, i):
    if i == k:
        return NF - 1
    return k if k < i <= k + SLOTS else k + SLOTS


def build(nc, dense, ids, ids_rows, tables, consts, w1z, w1d, b1, w2, b2, w3, z_dram, out):
    f32, f32r, i32 = mybir.dt.float32, mybir.dt.float32r, mybir.dt.int32
    ALU, ACT = mybir.AluOpType, mybir.ActivationFunctionType

    steps = [("dense",)] + [("onehot", j) for j in range(N_ONEHOT)]
    for t in range(TILES):
        steps += [("group", t, g) for g in range(len(GROUPS))] + [("gram", t)]
        if t:
            steps.append(("mlp", t - 1))
    steps.append(("mlp", TILES - 1))
    moves = [s for s in steps if s[0] in ("dense", "onehot", "group")]
    by_dve = [n for n, s in enumerate(moves) if s[0] == "group" and s[2] % 2 == 0]

    with ExitStack() as ctx:
        def sb(name, shape, dt=f32):
            return ctx.enter_context(nc.sbuf_tensor(name, shape, dt))

        def sem(name):
            return ctx.enter_context(nc.semaphore(name))

        ids_sb = sb("ids_sb", [P, TILES, len(ROWS)], i32)
        const_sb = sb("const_sb", [P, C_END])
        dense_sb = sb("dense_sb", [P, TILES, D])
        dense_t = sb("dense_t", [D, TILES, P])
        emb = sb("emb", [P, TILES, len(GATHERED), D])
        cols = sb("cols", [D, TILES, P, NF])
        ids_row = sb("ids_row", [TR, 2, TILES * P], i32)
        table = sb("table", [TR, 2, KMAX, D])
        table_hi = sb("table_hi", [TR, 2, KMAX, D], f32r)
        table_lo = sb("table_lo", [TR, 2, KMAX, D], f32r)
        onehot = sb("onehot", [TR, OHB, KH, TILES * P], f32r)
        z = sb("z", [P, 2, SLOTS, QG])
        zt = sb("zt", [P, 2, ZC, P])
        w1z_sb = sb("w1z_sb", [P, ZC, H1])
        w1d_sb = sb("w1d_sb", [D, H1])
        w2_sb = sb("w2_sb", [P, N1, H2])
        b2_sb = sb("b2_sb", [P, N2])
        w3_sb = sb("w3_sb", [P, N2])
        h1 = sb("h1", [P, N1, P])
        h2 = sb("h2", [P, N2, P])
        y_sb = sb("y_sb", [P, TILES])

        def bank(name):
            return ctx.enter_context(nc.psum_tensor(name, [P, 512], f32))

        ring = [bank(f"ring{i}") for i in range(RING)]
        gram = [bank(f"gram{i}") for i in range(HALVES)]
        h1_ps = [bank(f"h1_ps{i}") for i in range(2)]
        h2_ps = [bank(f"h2_ps{i}") for i in range(N2)]
        ident = const_sb[:, C_ID:C_ID + P]

        s_ids, s_const, s_dense, s_w1, s_w2 = map(sem, ("s_ids", "s_const", "s_dense", "s_w1", "s_w2"))
        s_gather = [[sem(f"s_gather{t}_{g}") for g in range(len(GROUPS))] for t in range(TILES)]
        s_table = [sem(f"s_table{i}") for i in range(2)]
        s_hi, s_lo, s_oh = sem("s_hi"), sem("s_lo"), sem("s_oh")
        s_ohused = sem("s_ohused")
        s_full = sem("s_full")
        s_act, s_dve = sem("s_act"), sem("s_dve")
        s_clear = sem("s_clear")
        s_ones = sem("s_ones")
        s_gram = sem("s_gram")
        s_near, s_far, s_z = sem("s_near"), sem("s_far"), sem("s_z")
        s_store = [sem(f"s_store{i}") for i in range(2)]
        s_zt = [sem(f"s_zt{i}") for i in range(2)]
        s_h1m, s_h1 = sem("s_h1m"), sem("s_h1")
        s_h1d = sem("s_h1d")
        s_h2m, s_h2, s_h2d = sem("s_h2m"), sem("s_h2"), sem("s_h2d")
        s_ym, s_y, s_out = sem("s_ym"), sem("s_y"), sem("s_out")

        def empties(n):
            if n in by_dve:
                return s_dve, by_dve.index(n) + 1
            return s_act, n + 1 - len([m for m in by_dve if m < n])

        def filled(n):
            if moves[n][0] == "onehot":
                return s_ohused, 2 * (moves[n][1] + 1)
            return s_full, len([m for m in moves[:n + 1] if m[0] != "onehot"])

        def ktiles(j):
            return ROWS[ONEHOT[j]] // TR

        def column_out(n):
            s = moves[n]
            if s[0] == "group":
                at = 1 + N_ONEHOT + GRP * s[2]
                return cols[:, s[1], :, at:at + len(GROUPS[s[2]])].rearrange("d p f -> d f p")
            return cols[:, :, :, 0 if s[0] == "dense" else 1 + s[1]]

        def column_in(n):
            s = moves[n]
            if s[0] == "group":
                k = len(GROUPS[s[2]])
                return ring[n % RING][:, 0:k * P].rearrange("d (f p) -> d f p", p=P)
            return ring[n % RING][:, :].rearrange("d (t p) -> d t p", p=P)

        def z_rows(t):
            return z_dram[t].rearrange("(k i) (q g) -> q i k g", i=NF, q=QUADS)

        block = ctx.enter_context(nc.Block())

        @block.sync
        def _(sp):
            sp.dma_start(ids_sb[:], ids).then_inc(s_ids, 16)
            sp.dma_start(const_sb[:], consts).then_inc(s_const, 16)
            sp.dma_start(dense_sb[:], dense.rearrange("(p t) d -> p t d", t=TILES)).then_inc(s_dense, 16)

            def load_table(j):
                k = ktiles(j)
                if j >= 2:
                    sp.wait_ge(s_lo, j - 1)
                    sp.wait_ge(s_oh, 2 * (j - 1))
                sp.dma_start(table[:, j % 2, 0:k, :],
                             tables[ONEHOT[j]].rearrange("(p k) d -> p k d", k=k)).then_inc(s_table[j % 2], 16)
                sp.dma_start(ids_row[:, j % 2, :],
                             ids_rows[ONEHOT[j]:ONEHOT[j] + 1, :].to_broadcast([TR, TILES * P])
                             ).then_inc(s_table[j % 2], 16)

            for j in range(N_ONEHOT // 2):
                load_table(j)
            sp.dma_start(w1z_sb[0:ZP, :, :], w1z).then_inc(s_w1, 16)
            sp.dma_start(w1z_sb[ZP:ZP + 1, 0, :], b1).then_inc(s_w1, 16)
            sp.dma_start(w1d_sb[:], w1d).then_inc(s_w1, 16)
            sp.dma_start(w2_sb[:], w2.rearrange("(k p) n -> p k n", p=P)).then_inc(s_w2, 16)
            sp.dma_start(b2_sb[:], b2).then_inc(s_w2, 16)
            sp.dma_start(w3_sb[:], w3).then_inc(s_w2, 16)
            for j in range(N_ONEHOT // 2, N_ONEHOT):
                load_table(j)
            sp.wait_ge(s_ones, 1)
            for t in range(TILES):
                sp.wait_ge(s_z, HALVES * (t + 1))
                for q in range(QUADS):
                    sp.dma_start(z_rows(t)[q], z[32 * q:32 * q + NF, t % 2]).then_inc(s_store[t % 2], 16)
                sp.wait_ge(s_store[t % 2], 16 * QUADS * (t // 2 + 1))
                if t >= 2:
                    sp.wait_ge(s_h1m, 2 * (t - 1))
                sp.dma_start(zt[0:ZP, t % 2], z_dram[t].rearrange("(c p) b -> p c b", p=ZP)
                             ).then_inc(s_zt[t % 2], 16)
            sp.wait_ge(s_y, TILES)
            sp.dma_start(out.rearrange("(p t) o -> p (t o)", t=TILES), y_sb[:]).then_inc(s_out, 16)
            sp.wait_ge(s_out, 16)

        @block.gpsimd
        def _(pool):
            pool.wait_ge(s_ids, 16)
            for t in range(TILES):
                for n, f in enumerate(GATHERED):
                    nc.gpsimd.indirect_dma_start(
                        emb[:, t, n, :], None, tables[f],
                        bass.IndirectOffsetOnAxis(ap=ids_sb[:, t, f:f + 1], axis=0),
                    ).then_inc(s_gather[t][n // GRP], 16)

        @block.tensor
        def _(pe):
            n = 0

            def claim():
                if n >= RING:
                    pe.wait_ge(*empties(n - RING))

            pe.wait_ge(s_const, 16)
            for s in steps:
                if s[0] == "dense":
                    pe.wait_ge(s_dense, 16)
                    for t in range(TILES):
                        last = nc.tensor.transpose(ring[0][:, t * P:(t + 1) * P], dense_sb[:, t, :], ident)
                    last.then_inc(s_full, 1)
                    n += 1
                elif s[0] == "onehot":
                    j, k = s[1], ktiles(s[1])
                    claim()
                    pe.wait_ge(s_hi, j + 1)
                    pe.wait_ge(s_lo, j + 1)
                    for half in range(2):
                        pe.wait_ge(s_oh, 2 * j + half + 1)
                        for c in range(k // 2):
                            row = half * (k // 2) + c
                            for part in (table_hi, table_lo):
                                last = nc.tensor.matmul(
                                    ring[n % RING][:, :], part[:, j % 2, row, :],
                                    onehot[:, (2 * j + half) % OHB, c, :],
                                    start=(row == 0 and part is table_hi),
                                    stop=(row == k - 1 and part is table_lo))
                        if half == 0:
                            last.then_inc(s_ohused, 1)
                    last.then_inc(s_ohused, 1)
                    n += 1
                elif s[0] == "group":
                    _, t, g = s
                    claim()
                    pe.wait_ge(s_gather[t][g], 16 * len(GROUPS[g]))
                    for i in range(len(GROUPS[g])):
                        last = nc.tensor.transpose(ring[n % RING][:, i * P:(i + 1) * P],
                                                   emb[:, t, GRP * g + i, :], ident)
                    last.then_inc(s_full, 1)
                    n += 1
                elif s[0] == "gram":
                    t = s[1]
                    at = max(m for m in range(len(moves)) if moves[m][:2] == ("group", t))
                    for engine in (True, False):
                        pe.wait_ge(*empties(max(m for m in range(at + 1) if (m in by_dve) == engine)))
                    if t == 0:
                        pe.wait_ge(s_clear, 1)
                    for half in range(HALVES):
                        if t:
                            pe.wait_ge(s_z, HALVES * (t - 1) + half + 1)
                        for g in range(GH):
                            for q in range(QUADS):
                                x = cols[:, t, QG * q + GH * half + g, :]
                                last = nc.tensor.matmul(
                                    gram[half][32 * q:32 * q + NF, NF * g:NF * (g + 1)], x, x,
                                    start=True, stop=True, tile_position=(0, 32 * q))
                        last.then_inc(s_gram, 1)
                else:
                    t = s[1]
                    if t == 0:
                        pe.wait_ge(s_w1, 48)
                        pe.wait_ge(s_w2, 48)
                    pe.wait_ge(s_zt[t % 2], 16 * (t // 2 + 1))
                    if t:
                        pe.wait_ge(s_h1, t)
                        pe.wait_ge(s_h1d, t)
                    for m in range(N1):
                        o = h1_ps[m // 2][:, (m % 2) * P:(m % 2 + 1) * P]
                        for c in range(ZC):
                            k = ZP + 1 if c == 0 else ZP
                            nc.tensor.matmul(o, w1z_sb[0:k, c, m * P:(m + 1) * P], zt[0:k, t % 2, c, :],
                                             start=(c == 0), stop=False)
                        last = nc.tensor.matmul(o, w1d_sb[:, m * P:(m + 1) * P], dense_t[:, t, :],
                                                start=False, stop=True)
                        if m % 2:
                            last.then_inc(s_h1m, 1)
                    for m in range(N2):
                        if m == 0 and t:
                            pe.wait_ge(s_h2, t)
                            pe.wait_ge(s_h2d, t)
                            pe.wait_ge(s_y, t)
                        for c in range(N1):
                            if m == 0 and c == 0:
                                pe.wait_ge(s_h1, t + 1)
                            if m == 0 and c == 2:
                                pe.wait_ge(s_h1d, t + 1)
                            last = nc.tensor.matmul(h2_ps[m][:, 0:P], w2_sb[:, c, m * P:(m + 1) * P],
                                                    h1[:, c, :], start=(c == 0), stop=(c == N1 - 1))
                        last.then_inc(s_h2m, 1)
                    for m in range(N2):
                        pe.wait_ge(*((s_h2, t + 1) if m == 0 else (s_h2d, t + 1)))
                        last = nc.tensor.matmul(h2_ps[0][:, P:P + 1], h2[:, m, :], w3_sb[:, m:m + 1],
                                                start=(m == 0), stop=(m == N2 - 1))
                    last.then_inc(s_ym, 1)

        @block.scalar
        def _(act):
            def part_hi(j):
                act.wait_ge(s_table[j % 2], 32 * (j // 2 + 1))
                if j >= 2:
                    act.wait_ge(s_ohused, 2 * (j - 1))
                nc.scalar.activation(table_hi[:, j % 2, 0:ktiles(j), :], table[:, j % 2, 0:ktiles(j), :],
                                     ACT.Copy).then_inc(s_hi, 1)

            part_hi(0)
            n = 0
            for s in steps:
                if s in moves:
                    if s[0] == "dense":
                        act.wait_ge(s_full, n + 1)
                        nc.scalar.activation(dense_t[:], column_in(n), ACT.Copy)
                    if s[0] == "onehot" and s[1] + 1 < N_ONEHOT:
                        part_hi(s[1] + 1)
                    if n not in by_dve:
                        act.wait_ge(*filled(n))
                        nc.scalar.activation(column_out(n), column_in(n), ACT.Copy).then_inc(s_act, 1)
                    n += 1
                elif s[0] == "mlp":
                    t = s[1]
                    act.wait_ge(s_h1m, 2 * t + 1)
                    if t:
                        act.wait_ge(s_h2m, N2 * t)
                    nc.scalar.activation(h1[:, 0:2, :], h1_ps[0][:, 0:2 * P].rearrange("p (m b) -> p m b", b=P),
                                         ACT.Relu).then_inc(s_h1, 1)
                    act.wait_ge(s_h2m, N2 * t + 1)
                    if t:
                        act.wait_ge(s_ym, t)
                    nc.scalar.activation(h2[:, 0, :], h2_ps[0][:, 0:P], ACT.Relu,
                                         bias=b2_sb[:, 0:1]).then_inc(s_h2, 1)

        @block.vector
        def _(dve):
            for half in range(HALVES):
                last = nc.vector.memset(gram[half][:, :], 0.0)
            last.then_inc(s_clear, 1)
            nc.vector.memset(zt[96:P, :, :, :], 1.0).then_inc(s_ones, 1)
            dve.wait_ge(s_const, 16)

            def prepare(j):
                k = ktiles(j)
                dve.wait_ge(s_table[j % 2], 32 * (j // 2 + 1))
                rows = C_ROW8 if k == 8 else C_ROW10
                for half in range(2):
                    h = 2 * j + half
                    if h >= OHB:
                        dve.wait_ge(s_ohused, h - OHB + 1)
                    for c in range(k // 2):
                        row = half * (k // 2) + c
                        last = nc.vector.tensor_scalar(
                            onehot[:, h % OHB, c, :], ids_row[:, j % 2, :],
                            const_sb[0:TR, rows + row:rows + row + 1], None, ALU.is_equal)
                    last.then_inc(s_oh, 1)
                    if half == 0:
                        dve.wait_ge(s_hi, j + 1)
                        if j >= 2:
                            dve.wait_ge(s_ohused, 2 * (j - 1))
                        nc.vector.tensor_tensor(table_lo[:, j % 2, 0:k, :], table[:, j % 2, 0:k, :],
                                                table_hi[:, j % 2, 0:k, :].bitcast(f32),
                                                ALU.subtract).then_inc(s_lo, 1)

            n = 0
            for s in steps:
                if s[0] == "onehot":
                    prepare(s[1])
                if s in moves:
                    if n in by_dve:
                        dve.wait_ge(*filled(n))
                        nc.vector.tensor_copy(column_out(n), column_in(n)).then_inc(s_dve, 1)
                    n += 1
                elif s[0] == "gram":
                    t = s[1]
                    if t >= 2:
                        dve.wait_ge(s_store[t % 2], 16 * QUADS * (t // 2))
                    for half in range(HALVES):
                        dve.wait_ge(s_gram, HALVES * t + half + 1)
                        g = gram[half][:, 0:GH * NF].rearrange("p (g j) -> p j g", j=NF)
                        o = z[:, t % 2, :, GH * half:GH * (half + 1)]
                        nc.vector.tensor_copy(o, g[:, 0:SLOTS, :]).then_inc(s_near, 1)
                        dve.wait_ge(s_near, HALVES * t + half + 1)
                        nc.vector.copy_predicated(
                            o, const_sb[:, C_FAR:C_FAR + SLOTS].bitcast(i32).unsqueeze(2).to_broadcast([P, SLOTS, GH]),
                            g[:, SLOTS:2 * SLOTS, :]).then_inc(s_far, 1)
                        dve.wait_ge(s_far, HALVES * t + half + 1)
                        nc.vector.copy_predicated(
                            o, const_sb[:, C_LAST:C_LAST + SLOTS].bitcast(i32).unsqueeze(2).to_broadcast([P, SLOTS, GH]),
                            g[:, NF - 1:NF, :].to_broadcast([P, SLOTS, GH])).then_inc(s_z, 1)
                elif s[0] == "mlp":
                    t = s[1]
                    dve.wait_ge(s_h1m, 2 * t + 2)
                    if t:
                        dve.wait_ge(s_h2m, N2 * t)
                    nc.vector.tensor_scalar(h1[:, 2:4, :], h1_ps[1][:, 0:2 * P].rearrange("p (m b) -> p m b", b=P),
                                            0.0, None, ALU.max).then_inc(s_h1d, 1)
                    dve.wait_ge(s_h2m, N2 * t + 2)
                    if t:
                        dve.wait_ge(s_ym, t)
                    nc.vector.tensor_scalar(h2[:, 1, :], h2_ps[1][:, 0:P], b2_sb[:, 1:2], 0.0,
                                            ALU.add, ALU.max).then_inc(s_h2d, 1)
                    dve.wait_ge(s_ym, t + 1)
                    nc.vector.tensor_copy(y_sb[:, t:t + 1], h2_ps[0][:, P:P + 1]).then_inc(s_y, 1)


def kernel(**inputs):
    import numpy as np
    import concourse.bacc as bacc
    from concourse.bass_utils import run_bass_kernel_spmd

    nc = bacc.Bacc("TRN2", target_bir_lowering=False, num_devices=1)
    arrays = {}

    def given(name, a):
        arrays[name] = a = np.ascontiguousarray(a)
        return nc.dram_tensor(name, a.shape, mybir.dt.from_np(a.dtype), kind="ExternalInput").ap()

    ids = np.asarray(inputs["ids"]).reshape(P, TILES, len(ROWS))
    w1 = np.asarray(inputs["W_top1"])
    iu, ju = np.triu_indices(NF, k=1)
    row_of = {(int(a), int(b)): r for r, (a, b) in enumerate(zip(iu, ju))}
    pair_rows = []
    consts = np.zeros((P, C_END), np.float32)
    consts[:, C_ID:C_ID + P] = np.eye(P)
    consts[:, C_ROW8:C_ROW8 + 8] = np.arange(P * 8).reshape(P, 8)
    consts[:, C_ROW10:C_ROW10 + 10] = np.arange(P * 10).reshape(P, 10)
    for k in range(SLOTS):
        for i in range(NF):
            j = partner(k, i)
            a, b = sorted((ORDER[i], ORDER[j]))
            pair_rows.append(row_of[a, b])
            at = {k: None, k + SLOTS: C_FAR, NF - 1: C_LAST}[j] if i != k else C_LAST
            if at is not None:
                consts[i::32, at + k] = 1.0
    args = [
        given("dense", inputs["r_dense_features"]),
        given("ids", ids),
        given("ids_rows", ids.transpose(2, 1, 0).reshape(len(ROWS), TILES * P)),
        [given(f"tbl_{f}", inputs[f"tbl_{f}"]) for f in range(len(ROWS))],
        given("consts", consts),
        given("w1z", w1[pair_rows].reshape(ZC, ZP, H1).transpose(1, 0, 2)),
        given("w1d", w1[NPAIR:]),
        given("b1", np.asarray(inputs["b_top1"]).reshape(1, H1)),
        given("w2", inputs["W_top2"]),
        given("b2", np.asarray(inputs["b_top2"]).reshape(N2, P).T),
        given("w3", np.asarray(inputs["W_top3"]).reshape(N2, P).T),
        nc.dram_tensor("z_dram", (TILES, NPAIR, P), mybir.dt.float32, kind="Internal").ap(),
        nc.dram_tensor("y", (TILES * P, 1), mybir.dt.float32, kind="ExternalOutput").ap(),
    ]
    build(nc, *args)
    r = run_bass_kernel_spmd(nc, [arrays], core_ids=[0])
    return r.results[0]["y"]
```

```python
import concourse.bass as bass
from concourse import mybir
from contextlib import ExitStack

P = 128
D = 128
TILES = 4
NF = 27
SLOTS = (NF - 1) // 2
NPAIR = NF * SLOTS
ZC = 3
ZP = NPAIR // ZC
H1, H2 = 512, 256
N1, N2 = H1 // P, H2 // P
QUADS = 4
QG = P // QUADS
HALVES = 2
GH = QG // HALVES
TR = 125
ROWS = [1000, 1000, 12500, 125000, 1000, 1250, 12500, 1000, 12500, 12500, 1250, 12500, 1000, 1250,
        1250, 1000, 1000, 12500, 12500, 1250, 1250, 12500, 1250, 1000, 1000, 1250]
N_ONEHOT = 9
ONEHOT = sorted(range(len(ROWS)), key=lambda f: ROWS[f])[:N_ONEHOT]
GATHERED = [f for f in range(len(ROWS)) if f not in ONEHOT]
ORDER = [0] + [1 + f for f in ONEHOT + GATHERED]
GRP = 4
GROUPS = [GATHERED[i:i + GRP] for i in range(0, len(GATHERED), GRP)]
KMAX = max(ROWS[f] for f in ONEHOT) // TR
KH = KMAX // 2
TB = 3
RING = 2
GATHERS_PER_TABLE, GATHERS_AHEAD = 3.3, 4
OHB = 4

C_ID = 0
C_ROW = C_ID + P
C_NEG = C_ROW + 18
C_FAR = C_NEG + 18
C_LAST = C_FAR + SLOTS
C_END = C_LAST + SLOTS


def row_at(k, row, base):
    at = base + (0 if k == 8 else 8) + row
    return slice(at, at + 1)


def partner(k, i):
    if i == k:
        return NF - 1
    return k if k < i <= k + SLOTS else k + SLOTS


def build(nc, dense, ids, ids_rows, tables, consts, w1z, w1d, b1, w2, b2, w3, z_dram, out):
    f32, f32r, i32 = mybir.dt.float32, mybir.dt.float32r, mybir.dt.int32
    ALU, ACT = mybir.AluOpType, mybir.ActivationFunctionType

    groups = [("group", t, g) for t in range(TILES) for g in range(len(GROUPS))]
    steps = [("dense",)]
    for j in range(N_ONEHOT):
        steps.append(("onehot", j))
        while (groups[0][1] * len(GATHERED) + (groups[0][2] + 1) * GRP
               <= GATHERS_AHEAD + GATHERS_PER_TABLE * (j + 1)):
            steps.append(groups.pop(0))

    def take(t, n):
        while n and groups and groups[0][1] <= t:
            steps.append(groups.pop(0))
            n -= 1

    take(0, GRP)
    steps.append(("gram", 0, 0))
    take(1, 1)
    steps.append(("gram", 0, 1))
    take(1, NF)
    steps.append(("gram", 1, 0))
    take(2, 1)
    steps.append(("gram", 1, 1))
    take(2, 1)
    steps.append(("mlp1", 0))
    take(2, 1)
    steps.append(("mlp2", 0))
    take(2, 1)
    steps += [("mlp1", 1), ("mlp3", 0)]
    take(2, NF)
    steps += [("mlp2", 1), ("gram", 2, 0), ("mlp3", 1)]
    take(3, 1)
    steps.append(("gram", 2, 1))
    take(3, NF)
    steps += [("gram", 3, 0), ("gram", 3, 1), ("mlp1", 2), ("mlp2", 2), ("mlp3", 2)]
    steps += [("mlp1", 3), ("mlp2", 3), ("mlp3", 3)]
    moves = [s for s in steps if s[0] in ("dense", "onehot", "group")]
    EARLY = len([s for s in steps[:steps.index(("gram", 0, 0))] if s in moves])
    by_dve = [n for n, s in enumerate(moves) if s[0] == "group" and s[2] % 2 == 0]

    with ExitStack() as ctx:
        def sb(name, shape, dt=f32):
            return ctx.enter_context(nc.sbuf_tensor(name, shape, dt))

        def sem(name):
            return ctx.enter_context(nc.semaphore(name))

        ids_sb = sb("ids_sb", [P, TILES, len(ROWS)], i32)
        const_sb = sb("const_sb", [P, C_END])
        dense_sb = sb("dense_sb", [P, TILES, D])
        dense_t = sb("dense_t", [D, TILES, P])
        emb = sb("emb", [P, TILES, len(GATHERED), D])
        cols = sb("cols", [D, TILES, P, NF])
        ids_row = sb("ids_row", [P, TB, TILES * P], i32)
        table = sb("table", [TR, TB, KMAX, D])
        table_hi = sb("table_hi", [TR, 2, KMAX, D], f32r)
        table_lo = sb("table_lo", [TR, 2, KMAX, D], f32r)
        onehot = sb("onehot", [TR, OHB, KH, TILES * P], f32r)
        distance = sb("distance", [TR, 2, TILES * P])
        z = sb("z", [P, 2, SLOTS, QG])
        zt = sb("zt", [P, 2, ZC, P])
        w1z_sb = sb("w1z_sb", [P, ZC, H1])
        w1d_sb = sb("w1d_sb", [D, H1])
        w2_sb = sb("w2_sb", [P, N1, H2])
        b2_sb = sb("b2_sb", [P, N2])
        w3_sb = sb("w3_sb", [P, N2])
        h1 = sb("h1", [P, N1, P])
        h2 = sb("h2", [P, N2, P])
        y_sb = sb("y_sb", [P, TILES])

        def bank(name):
            return ctx.enter_context(nc.psum_tensor(name, [P, 512], f32))

        ring = [bank(f"ring{i}") for i in range(RING)]
        gram = [bank(f"gram{i}") for i in range(HALVES)]
        h1_ps = [bank(f"h1_ps{i}") for i in range(2)]
        h2_ps = [bank(f"h2_ps{i}") for i in range(N2)]
        ident = const_sb[:, C_ID:C_ID + P]

        s_ids, s_const, s_dense, s_w1, s_w2 = map(sem, ("s_ids", "s_const", "s_dense", "s_w1", "s_w2"))
        s_gather = [[sem(f"s_gather{t}_{g}") for g in range(len(GROUPS))] for t in range(TILES)]
        s_table = [sem(f"s_table{i}") for i in range(TB)]
        s_idrow = [sem(f"s_idrow{i}") for i in range(TB)]
        s_hi, s_lo, s_oh = sem("s_hi"), sem("s_lo"), sem("s_oh")
        s_dist, s_oha = sem("s_dist"), sem("s_oha")
        s_ohused = sem("s_ohused")
        s_full = sem("s_full")
        s_act, s_dve = sem("s_act"), sem("s_dve")
        s_clear = sem("s_clear")
        s_ones = sem("s_ones")
        s_gram = sem("s_gram")
        s_near, s_far, s_z = sem("s_near"), sem("s_far"), sem("s_z")
        s_store = [sem(f"s_store{i}") for i in range(2)]
        s_zt = [sem(f"s_zt{i}") for i in range(2)]
        s_h1m, s_h1 = sem("s_h1m"), sem("s_h1")
        s_h1d = sem("s_h1d")
        s_h2m, s_h2, s_h2d = sem("s_h2m"), sem("s_h2"), sem("s_h2d")
        s_ym, s_y, s_out = sem("s_ym"), sem("s_y"), sem("s_out")

        def bank_of(n):
            if n < EARLY:
                return (ring + h1_ps)[n % (RING + 2)]
            return ring[(n - EARLY) % RING]

        def bank_free(n):
            at = max((m for m in range(n) if bank_of(m) is bank_of(n)), default=None)
            return None if at is None else empties(at)

        def empties(n):
            if n in by_dve:
                return s_dve, by_dve.index(n) + 1
            return s_act, n + 1 - len([m for m in by_dve if m < n])

        def filled(n):
            if moves[n][0] == "onehot":
                return s_ohused, 2 * (moves[n][1] + 1)
            return s_full, len([m for m in moves[:n + 1] if m[0] != "onehot"])

        def ktiles(j):
            return ROWS[ONEHOT[j]] // TR

        def column_out(n):
            s = moves[n]
            if s[0] == "group":
                at = 1 + N_ONEHOT + GRP * s[2]
                return cols[:, s[1], :, at:at + len(GROUPS[s[2]])].rearrange("d p f -> d f p")
            return cols[:, :, :, 0 if s[0] == "dense" else 1 + s[1]]

        def column_in(n):
            s = moves[n]
            if s[0] == "group":
                k = len(GROUPS[s[2]])
                return bank_of(n)[:, 0:k * P].rearrange("d (f p) -> d f p", p=P)
            return bank_of(n)[:, :].rearrange("d (t p) -> d t p", p=P)

        def z_rows(t):
            return z_dram[t].rearrange("(k i) (q g) -> q i k g", i=NF, q=QUADS)

        block = ctx.enter_context(nc.Block())

        @block.sync
        def _(sp):
            def load_table(j):
                k = ktiles(j)
                if j >= TB:
                    sp.wait_ge(s_lo, j - TB + 1)
                    sp.wait_ge(s_oh, 2 * (j - TB + 1))
                    sp.wait_ge(s_oha, 2 * (j - TB + 1))
                sp.dma_start(ids_row[:, j % TB, :],
                             ids_rows[ONEHOT[j]:ONEHOT[j] + 1, :].to_broadcast([P, TILES * P])
                             ).then_inc(s_idrow[j % TB], 16)
                rows = tables[ONEHOT[j]].rearrange("(p k) d -> p k d", k=k)
                for a, b in ((0, TR // 16 * 16), (TR // 16 * 16, TR)):
                    sp.dma_start(table[a:b, j % TB, 0:k, :], rows[a:b]).then_inc(s_table[j % TB], 16)

            for j in range(N_ONEHOT // 2):
                load_table(j)
            sp.dma_start(w1z_sb[0:ZP, :, :], w1z).then_inc(s_w1, 16)
            sp.dma_start(w1z_sb[ZP:ZP + 1, 0, :], b1).then_inc(s_w1, 16)
            sp.dma_start(w1d_sb[:], w1d).then_inc(s_w1, 16)
            sp.dma_start(w2_sb[:], w2.rearrange("(k p) n -> p k n", p=P)).then_inc(s_w2, 16)
            sp.dma_start(b2_sb[:], b2).then_inc(s_w2, 16)
            sp.dma_start(w3_sb[:], w3).then_inc(s_w2, 16)
            for j in range(N_ONEHOT // 2, N_ONEHOT):
                load_table(j)
            sp.wait_ge(s_ones, 1)
            for t in range(TILES):
                sp.wait_ge(s_z, HALVES * (t + 1))
                for q in (range(QUADS) if t < TILES - 1 else range(QUADS // 2)):
                    sp.dma_start(z_rows(t)[q], z[32 * q:32 * q + NF, t % 2]).then_inc(s_store[t % 2], 16)
                sp.wait_ge(s_store[t % 2], 16 * QUADS * (t // 2 + 1))
                if t >= 2:
                    sp.wait_ge(s_h1m, 2 * (t - 1))
                sp.dma_start(zt[0:ZP, t % 2], z_dram[t].rearrange("(c p) b -> p c b", p=ZP)
                             ).then_inc(s_zt[t % 2], 16)
            sp.wait_ge(s_y, TILES)
            sp.dma_start(out.rearrange("(p t) o -> p (t o)", t=TILES), y_sb[:]).then_inc(s_out, 16)
            sp.wait_ge(s_out, 16)

        @block.gpsimd
        def _(pool):
            pool.wait_ge(s_ids, 16)
            for t in range(TILES):
                for n, f in enumerate(GATHERED):
                    nc.gpsimd.indirect_dma_start(
                        emb[:, t, n, :], None, tables[f],
                        bass.IndirectOffsetOnAxis(ap=ids_sb[:, t, f:f + 1], axis=0),
                    ).then_inc(s_gather[t][n // GRP], 16)

        @block.tensor
        def _(pe):
            n = 0

            def claim():
                if bank_free(n):
                    pe.wait_ge(*bank_free(n))

            pe.wait_ge(s_const, 16)
            for s in steps:
                if s[0] == "dense":
                    pe.wait_ge(s_dense, 16)
                    for t in range(TILES):
                        last = nc.tensor.transpose(bank_of(0)[:, t * P:(t + 1) * P], dense_sb[:, t, :], ident)
                    last.then_inc(s_full, 1)
                    n += 1
                elif s[0] == "onehot":
                    j, k = s[1], ktiles(s[1])
                    claim()
                    pe.wait_ge(s_hi, j + 1)
                    pe.wait_ge(s_lo, j + 1)
                    for half in range(2):
                        pe.wait_ge(s_oh, 2 * j + half + 1)
                        for c in range(k // 2):
                            if c == k // 2 - 1:
                                pe.wait_ge(s_oha, 2 * j + half + 1)
                            row = half * (k // 2) + c
                            for part in (table_hi, table_lo):
                                last = nc.tensor.matmul(
                                    bank_of(n)[:, :], part[:, j % 2, row, :],
                                    onehot[:, (2 * j + half) % OHB, c, :],
                                    start=(row == 0 and part is table_hi),
                                    stop=(row == k - 1 and part is table_lo))
                        if half == 0:
                            last.then_inc(s_ohused, 1)
                    last.then_inc(s_ohused, 1)
                    n += 1
                elif s[0] == "group":
                    _, t, g = s
                    claim()
                    pe.wait_ge(s_gather[t][g], 16 * len(GROUPS[g]))
                    for i in range(len(GROUPS[g])):
                        last = nc.tensor.transpose(bank_of(n)[:, i * P:(i + 1) * P],
                                                   emb[:, t, GRP * g + i, :], ident)
                    last.then_inc(s_full, 1)
                    n += 1
                elif s[0] == "gram":
                    _, t, half = s
                    if half == 0:
                        at = max(moves.index(("onehot", N_ONEHOT - 1)),
                                 moves.index(("group", t, len(GROUPS) - 1)))
                        for engine in (True, False):
                            pe.wait_ge(*empties(max(m for m in range(at + 1) if (m in by_dve) == engine)))
                    if t == 0:
                        pe.wait_ge(s_clear, 1)
                    else:
                        pe.wait_ge(s_z, HALVES * (t - 1) + half + 1)
                    for g in range(GH):
                        for q in range(QUADS):
                            x = cols[:, t, QG * q + GH * half + g, :]
                            last = nc.tensor.matmul(
                                gram[half][32 * q:32 * q + NF, NF * g:NF * (g + 1)], x, x,
                                start=True, stop=True, tile_position=(0, 32 * q))
                    last.then_inc(s_gram, 1)
                elif s[0] == "mlp1":
                    t = s[1]
                    if t == 0:
                        pe.wait_ge(s_w1, 48)
                        pe.wait_ge(s_w2, 48)
                    if t:
                        pe.wait_ge(s_h1, t)
                        pe.wait_ge(s_h1d, t)
                    for m in range(N1):
                        o = h1_ps[m // 2][:, (m % 2) * P:(m % 2 + 1) * P]
                        nc.tensor.matmul(o, w1d_sb[:, m * P:(m + 1) * P], dense_t[:, t, :],
                                         start=(m % 2 == 0), stop=False, skip_group_check=True)
                    pe.wait_ge(s_zt[t % 2], 16 * (t // 2 + 1))
                    for m in range(N1):
                        o = h1_ps[m // 2][:, (m % 2) * P:(m % 2 + 1) * P]
                        for c in range(ZC):
                            k = ZP + 1 if c == 0 else ZP
                            last = nc.tensor.matmul(o, w1z_sb[0:k, c, m * P:(m + 1) * P],
                                                    zt[0:k, t % 2, c, :], start=False,
                                                    stop=(c == ZC - 1), skip_group_check=True)
                        if m % 2:
                            last.then_inc(s_h1m, 1)
                elif s[0] == "mlp2":
                    t = s[1]
                    for m in range(N2):
                        if m == 0 and t:
                            pe.wait_ge(s_h2, t)
                            pe.wait_ge(s_h2d, t)
                            pe.wait_ge(s_y, t)
                        for c in range(N1):
                            if m == 0 and c == 0:
                                pe.wait_ge(s_h1, t + 1)
                            if m == 0 and c == 2:
                                pe.wait_ge(s_h1d, t + 1)
                            last = nc.tensor.matmul(h2_ps[m][:, 0:P], w2_sb[:, c, m * P:(m + 1) * P],
                                                    h1[:, c, :], start=(c == 0), stop=(c == N1 - 1))
                        last.then_inc(s_h2m, 1)
                else:
                    t = s[1]
                    for m in range(N2):
                        pe.wait_ge(*((s_h2, t + 1) if m == 0 else (s_h2d, t + 1)))
                        last = nc.tensor.matmul(h2_ps[0][:, P:P + 1], h2[:, m, :], w3_sb[:, m:m + 1],
                                                start=(m == 0), stop=(m == N2 - 1))
                    last.then_inc(s_ym, 1)

        @block.scalar
        def _(act):
            act.dma_start(ids_sb[:], ids).then_inc(s_ids, 16)
            act.dma_start(const_sb[:], consts).then_inc(s_const, 16)
            act.dma_start(dense_sb[:], dense.rearrange("(p t) d -> p t d", t=TILES)).then_inc(s_dense, 16)

            def share(j):
                k = ktiles(j)
                act.wait_ge(s_idrow[j % TB], 16 * (j // TB + 1))
                if j:
                    act.wait_ge(s_oha, 2 * j)
                for half in range(2):
                    row = (half + 1) * (k // 2) - 1
                    nc.scalar.activation(distance[:, half, :], ids_row[0:TR, j % TB, :], ACT.Abs,
                                         bias=const_sb[0:TR, row_at(k, row, C_NEG)]).then_inc(s_dist, 1)
                for half in range(2):
                    h = 2 * j + half
                    if h >= OHB:
                        act.wait_ge(s_ohused, h - OHB + 1)
                    act.wait_ge(s_dist, h + 1)
                    nc.scalar.activation(onehot[:, h % OHB, k // 2 - 1, :], distance[:, half, :], ACT.Relu,
                                         bias=1.0, scale=-1.0).then_inc(s_oha, 1)

            def part_hi(j):
                act.wait_ge(s_table[j % TB], 32 * (j // TB + 1))
                if j >= 2:
                    act.wait_ge(s_ohused, 2 * (j - 1))
                nc.scalar.activation(table_hi[:, j % 2, 0:ktiles(j), :], table[:, j % TB, 0:ktiles(j), :],
                                     ACT.Copy).then_inc(s_hi, 1)

            part_hi(0)
            act.wait_ge(s_const, 16)
            share(0)
            n = 0
            for s in steps:
                if s in moves:
                    if s[0] == "dense":
                        act.wait_ge(s_full, n + 1)
                        nc.scalar.activation(dense_t[:], column_in(n), ACT.Copy)
                    if s[0] == "onehot" and s[1] + 1 < N_ONEHOT:
                        part_hi(s[1] + 1)
                        share(s[1] + 1)
                    if n not in by_dve:
                        act.wait_ge(*filled(n))
                        nc.scalar.activation(column_out(n), column_in(n), ACT.Copy).then_inc(s_act, 1)
                    n += 1
                elif s == ("gram", TILES - 1, HALVES - 1):
                    act.wait_ge(s_z, HALVES * TILES)
                    for q in range(QUADS // 2, QUADS):
                        act.dma_start(z_rows(s[1])[q], z[32 * q:32 * q + NF, s[1] % 2]).then_inc(s_store[s[1] % 2], 16)
                elif s[0] == "mlp1":
                    t = s[1]
                    act.wait_ge(s_h1m, 2 * t + 1)
                    if t:
                        act.wait_ge(s_h2m, N2 * t)
                    nc.scalar.activation(h1[:, 0:2, :], h1_ps[0][:, 0:2 * P].rearrange("p (m b) -> p m b", b=P),
                                         ACT.Relu).then_inc(s_h1, 1)
                elif s[0] == "mlp2":
                    t = s[1]
                    act.wait_ge(s_h2m, N2 * t + 1)
                    if t:
                        act.wait_ge(s_ym, t)
                    nc.scalar.activation(h2[:, 0, :], h2_ps[0][:, 0:P], ACT.Relu,
                                         bias=b2_sb[:, 0:1]).then_inc(s_h2, 1)

        @block.vector
        def _(dve):
            for half in range(HALVES):
                last = nc.vector.memset(gram[half][:, :], 0.0)
            last.then_inc(s_clear, 1)
            nc.vector.memset(zt[96:P, :, :, :], 1.0).then_inc(s_ones, 1)
            dve.wait_ge(s_const, 16)

            def prepare(j):
                k = ktiles(j)
                dve.wait_ge(s_table[j % TB], 32 * (j // TB + 1))
                dve.wait_ge(s_hi, j + 1)
                if j >= 2:
                    dve.wait_ge(s_ohused, 2 * (j - 1))
                nc.vector.tensor_tensor(table_lo[:, j % 2, 0:k, :], table[:, j % TB, 0:k, :],
                                        table_hi[:, j % 2, 0:k, :].bitcast(f32),
                                        ALU.subtract).then_inc(s_lo, 1)
                dve.wait_ge(s_idrow[j % TB], 16 * (j // TB + 1))
                for half in range(2):
                    h = 2 * j + half
                    if h >= OHB:
                        dve.wait_ge(s_ohused, h - OHB + 1)
                    for c in range(k // 2 - 1):
                        row = half * (k // 2) + c
                        last = nc.vector.tensor_scalar(
                            onehot[:, h % OHB, c, :], ids_row[0:TR, j % TB, :],
                            const_sb[0:TR, row_at(k, row, C_ROW)], None, ALU.is_equal)
                    last.then_inc(s_oh, 1)

            prepare(0)
            n = 0
            for s in steps:
                if s[0] == "onehot" and s[1] + 1 < N_ONEHOT:
                    prepare(s[1] + 1)
                if s in moves:
                    if n in by_dve:
                        dve.wait_ge(*filled(n))
                        nc.vector.tensor_copy(column_out(n), column_in(n)).then_inc(s_dve, 1)
                    n += 1
                elif s[0] == "gram":
                    _, t, half = s
                    if t >= 2:
                        dve.wait_ge(s_store[t % 2], 16 * QUADS * (t // 2))
                    dve.wait_ge(s_gram, HALVES * t + half + 1)
                    g = gram[half][:, 0:GH * NF].rearrange("p (g j) -> p j g", j=NF)
                    o = z[:, t % 2, :, GH * half:GH * (half + 1)]
                    far, last = (const_sb[:, c:c + SLOTS].bitcast(i32).unsqueeze(2).to_broadcast([P, SLOTS, GH])
                                 for c in (C_FAR, C_LAST))
                    nc.vector.tensor_copy(o, g[:, 0:SLOTS, :]).then_inc(s_near, 1)
                    dve.wait_ge(s_near, HALVES * t + half + 1)
                    nc.vector.copy_predicated(o, far, g[:, SLOTS:2 * SLOTS, :]).then_inc(s_far, 1)
                    dve.wait_ge(s_far, HALVES * t + half + 1)
                    nc.vector.copy_predicated(o, last, g[:, NF - 1:NF, :].to_broadcast([P, SLOTS, GH])
                                              ).then_inc(s_z, 1)
                elif s[0] == "mlp1":
                    t = s[1]
                    dve.wait_ge(s_h1m, 2 * t + 2)
                    if t:
                        dve.wait_ge(s_h2m, N2 * t)
                    nc.vector.tensor_scalar(h1[:, 2:4, :], h1_ps[1][:, 0:2 * P].rearrange("p (m b) -> p m b", b=P),
                                            0.0, None, ALU.max).then_inc(s_h1d, 1)
                elif s[0] == "mlp2":
                    t = s[1]
                    dve.wait_ge(s_h2m, N2 * t + 2)
                    if t:
                        dve.wait_ge(s_ym, t)
                    nc.vector.tensor_scalar(h2[:, 1, :], h2_ps[1][:, 0:P], b2_sb[:, 1:2], 0.0,
                                            ALU.add, ALU.max).then_inc(s_h2d, 1)
                elif s[0] == "mlp3":
                    t = s[1]
                    dve.wait_ge(s_ym, t + 1)
                    nc.vector.tensor_copy(y_sb[:, t:t + 1], h2_ps[0][:, P:P + 1]).then_inc(s_y, 1)


def kernel(**inputs):
    import numpy as np
    import concourse.bacc as bacc
    from concourse.bass_utils import run_bass_kernel_spmd

    nc = bacc.Bacc("TRN2", target_bir_lowering=False, num_devices=1)
    arrays = {}

    def given(name, a):
        arrays[name] = a = np.ascontiguousarray(a)
        return nc.dram_tensor(name, a.shape, mybir.dt.from_np(a.dtype), kind="ExternalInput").ap()

    ids = np.asarray(inputs["ids"]).reshape(P, TILES, len(ROWS))
    w1 = np.asarray(inputs["W_top1"])
    iu, ju = np.triu_indices(NF, k=1)
    row_of = {(int(a), int(b)): r for r, (a, b) in enumerate(zip(iu, ju))}
    pair_rows = []
    consts = np.zeros((P, C_END), np.float32)
    consts[:, C_ID:C_ID + P] = np.eye(P)
    rows = np.concatenate([np.arange(P * k).reshape(P, k) for k in (8, 10)], axis=1)
    consts[:, C_ROW:C_ROW + 18] = rows
    consts[:, C_NEG:C_NEG + 18] = -rows
    for k in range(SLOTS):
        for i in range(NF):
            j = partner(k, i)
            a, b = sorted((ORDER[i], ORDER[j]))
            pair_rows.append(row_of[a, b])
            at = {k: None, k + SLOTS: C_FAR, NF - 1: C_LAST}[j] if i != k else C_LAST
            if at is not None:
                consts[i::32, at + k] = 1.0
    args = [
        given("dense", inputs["r_dense_features"]),
        given("ids", ids),
        given("ids_rows", ids.transpose(2, 1, 0).reshape(len(ROWS), TILES * P)),
        [given(f"tbl_{f}", inputs[f"tbl_{f}"]) for f in range(len(ROWS))],
        given("consts", consts),
        given("w1z", w1[pair_rows].reshape(ZC, ZP, H1).transpose(1, 0, 2)),
        given("w1d", w1[NPAIR:]),
        given("b1", np.asarray(inputs["b_top1"]).reshape(1, H1)),
        given("w2", inputs["W_top2"]),
        given("b2", np.asarray(inputs["b_top2"]).reshape(N2, P).T),
        given("w3", np.asarray(inputs["W_top3"]).reshape(N2, P).T),
        nc.dram_tensor("z_dram", (TILES, NPAIR, P), mybir.dt.float32, kind="Internal").ap(),
        nc.dram_tensor("y", (TILES * P, 1), mybir.dt.float32, kind="ExternalOutput").ap(),
    ]
    build(nc, *args)
    r = run_bass_kernel_spmd(nc, [arrays], core_ids=[0])
    return r.results[0]["y"]
```

```python
import concourse.bass as bass
from concourse import mybir
from contextlib import ExitStack

P = 128
D = 128
TILES = 4
NF = 27
SLOTS = (NF - 1) // 2
NPAIR = NF * SLOTS
ZC = 3
ZP = NPAIR // ZC
H1, H2 = 512, 256
N1, N2 = H1 // P, H2 // P
QUADS = 4
QG = P // QUADS
HALVES = 2
GH = QG // HALVES
TR = 125
ROWS = [1000, 1000, 12500, 125000, 1000, 1250, 12500, 1000, 12500, 12500, 1250, 12500, 1000, 1250,
        1250, 1000, 1000, 12500, 12500, 1250, 1250, 12500, 1250, 1000, 1000, 1250]
N_ONEHOT = 10
ONEHOT = sorted(range(len(ROWS)), key=lambda f: ROWS[f])[:N_ONEHOT]
GATHERED = [f for f in range(len(ROWS)) if f not in ONEHOT]
ORDER = [0] + [1 + f for f in ONEHOT + GATHERED]
GRP = 4
GROUPS = [GATHERED[i:i + GRP] for i in range(0, len(GATHERED), GRP)]
KMAX = max(ROWS[f] for f in ONEHOT) // TR
KH = KMAX // 2
WARM = 11
TB = 3
RING = 2
SCHEDULE = """
    onehot onehot group onehot dense onehot group group onehot onehot group onehot group
    onehot onehot group group onehot group group gram group gram group gram group gram gram
    gram group mlp1 mlp2 group mlp1 mlp3 group group mlp2 gram gram mlp3 mlp1 mlp2 mlp3 mlp1
    mlp2 mlp3
"""
OHB = 4

C_ID = 0
C_ROW = C_ID + P
C_NEG = C_ROW + 18
C_FAR = C_NEG + 18
C_LAST = C_FAR + SLOTS
C_END = C_LAST + SLOTS


def row_at(k, row, base):
    at = base + (0 if k == 8 else 8) + row
    return slice(at, at + 1)


def partner(k, i):
    if i == k:
        return NF - 1
    return k if k < i <= k + SLOTS else k + SLOTS


def build(nc, dense, ids, ids_rows, tables, consts, w1z, w1d, b1, w2, b2, w3, z_dram, out):
    f32, f32r, i32 = mybir.dt.float32, mybir.dt.float32r, mybir.dt.int32
    ALU, ACT = mybir.AluOpType, mybir.ActivationFunctionType

    counts = {kind: 0 for kind in ("dense", "onehot", "group", "gram", "mlp1", "mlp2", "mlp3")}
    steps = []
    for kind in SCHEDULE.split():
        n = counts[kind]
        counts[kind] += 1
        of = {"dense": (), "group": divmod(n, len(GROUPS)), "gram": divmod(n, HALVES)}
        steps.append((kind, *of.get(kind, (n,))))
    moves = [s for s in steps if s[0] in ("dense", "onehot", "group")]
    EARLY = len([s for s in steps[:steps.index(("gram", 0, 0))] if s in moves])
    by_dve = [n for n, s in enumerate(moves) if s[0] == "group" and s[2] % 2 == 0]

    with ExitStack() as ctx:
        def sb(name, shape, dt=f32):
            return ctx.enter_context(nc.sbuf_tensor(name, shape, dt))

        def sem(name):
            return ctx.enter_context(nc.semaphore(name))

        ids_sb = sb("ids_sb", [P, TILES, len(ROWS)], i32)
        const_sb = sb("const_sb", [P, C_END])
        dense_sb = sb("dense_sb", [P, TILES, D])
        dense_t = sb("dense_t", [D, TILES, P])
        emb = sb("emb", [P, TILES, len(GATHERED), D])
        cols = sb("cols", [D, TILES, P, NF])
        ids_row = sb("ids_row", [P, TB, TILES * P], i32)
        table = sb("table", [TR, TB, KMAX, D])
        table_hi = sb("table_hi", [TR, 2, KMAX, D], f32r)
        table_lo = sb("table_lo", [TR, 2, KMAX, D], f32r)
        onehot = sb("onehot", [TR, OHB, KH, TILES * P], f32r)
        distance = sb("distance", [TR, 2, TILES * P])
        z = sb("z", [P, 2, SLOTS, QG])
        zt = sb("zt", [P, 2, QUADS, ZC, QG])
        w1z_sb = sb("w1z_sb", [P, ZC, H1])
        w1d_sb = sb("w1d_sb", [D, H1])
        w2_sb = sb("w2_sb", [P, N1, H2])
        b2_sb = sb("b2_sb", [P, N2])
        w3_sb = sb("w3_sb", [P, N2])
        h1 = sb("h1", [P, N1, P])
        h2 = sb("h2", [P, N2, P])
        y_sb = sb("y_sb", [P, TILES])
        warm = sb("warm", [P, 512], mybir.dt.bfloat16)
        unread = sb("unread", [1, 1])

        def bank(name):
            return ctx.enter_context(nc.psum_tensor(name, [P, 512], f32))

        ring = [bank(f"ring{i}") for i in range(RING)]
        gram = [bank(f"gram{i}") for i in range(HALVES)]
        h1_ps = [bank(f"h1_ps{i}") for i in range(2)]
        h2_ps = [bank(f"h2_ps{i}") for i in range(N2)]
        ident = const_sb[:, C_ID:C_ID + P]

        s_ids, s_const, s_dense, s_w1, s_w2 = map(sem, ("s_ids", "s_const", "s_dense", "s_w1", "s_w2"))
        s_gather = [[sem(f"s_gather{t}_{g}") for g in range(len(GROUPS))] for t in range(TILES)]
        s_table = [sem(f"s_table{i}") for i in range(TB)]
        s_idrow = [sem(f"s_idrow{i}") for i in range(TB)]
        s_hi0 = sem("s_hi0")
        s_hi, s_lo = sem("s_hi"), sem("s_lo")
        s_oh, s_oha = sem("s_oh"), sem("s_oha")
        s_dist = sem("s_dist")
        s_ohused = sem("s_ohused")
        s_full = sem("s_full")
        s_act, s_dve = sem("s_act"), sem("s_dve")
        s_warm = sem("s_warm")
        s_clear = sem("s_clear")
        s_ones = sem("s_ones")
        s_gram = sem("s_gram")
        s_near, s_far, s_z = sem("s_near"), sem("s_far"), sem("s_z")
        s_store = [sem(f"s_store{i}") for i in range(2)]
        s_zt = [sem(f"s_zt{i}") for i in range(2)]
        s_h1m, s_h1 = sem("s_h1m"), sem("s_h1")
        s_h1d = sem("s_h1d")
        s_h2m, s_h2, s_h2d = sem("s_h2m"), sem("s_h2"), sem("s_h2d")
        s_ym, s_y, s_out = sem("s_ym"), sem("s_y"), sem("s_out")

        def bank_of(n):
            if n < EARLY:
                return (ring + h1_ps)[n % (RING + 2)]
            return ring[(n - EARLY) % RING]

        def bank_free(n):
            at = max((m for m in range(n) if bank_of(m) is bank_of(n)), default=None)
            return None if at is None else empties(at)

        def empties(n):
            if n in by_dve:
                return s_dve, by_dve.index(n) + 1
            return s_act, n + 1 - len([m for m in by_dve if m < n])

        def filled(n):
            if moves[n][0] == "onehot":
                return s_ohused, 2 * (moves[n][1] + 1)
            return s_full, len([m for m in moves[:n + 1] if m[0] != "onehot"])

        def high_part(j):
            return (s_hi, j) if j else (s_hi0, 1)

        def ktiles(j):
            return ROWS[ONEHOT[j]] // TR

        def column_out(n):
            s = moves[n]
            if s[0] == "group":
                at = 1 + N_ONEHOT + GRP * s[2]
                return cols[:, s[1], :, at:at + len(GROUPS[s[2]])].rearrange("d p f -> d f p")
            return cols[:, :, :, 0 if s[0] == "dense" else 1 + s[1]]

        def column_in(n):
            s = moves[n]
            if s[0] == "group":
                k = len(GROUPS[s[2]])
                return bank_of(n)[:, 0:k * P].rearrange("d (f p) -> d f p", p=P)
            return bank_of(n)[:, :].rearrange("d (t p) -> d t p", p=P)

        def pair_rows(t):
            rows = z_dram[t].rearrange("(q i) k g -> q (i k) g", q=QUADS)[:, 0:NPAIR]
            return rows.rearrange("q (p c) g -> p q (c g)", c=ZC)

        block = ctx.enter_context(nc.Block())

        @block.sync
        def _(sp):
            def load_ids_row(j):
                sp.dma_start(ids_row[:, j % TB, :],
                             ids_rows[ONEHOT[j]:ONEHOT[j] + 1, :].to_broadcast([P, TILES * P])
                             ).then_inc(s_idrow[j % TB], 16)

            def load_table(j):
                k = ktiles(j)
                if j >= TB:
                    sp.wait_ge(s_lo, j - TB + 1)
                    sp.wait_ge(s_oh, 2 * (j - TB + 1))
                    sp.wait_ge(s_oha, j - TB + 1)
                rows = tables[ONEHOT[j]].rearrange("(p k) d -> p k d", k=k)
                for a, b in ((0, TR // 16 * 16), (TR // 16 * 16, TR)):
                    sp.dma_start(table[a:b, j % TB, 0:k, :], rows[a:b]).then_inc(s_table[j % TB], 16)
                if j:
                    load_ids_row(j)

            sp.dma_start(ids_sb[:], ids).then_inc(s_ids, 16)
            load_ids_row(0)
            load_table(0)
            load_table(1)
            sp.dma_start(dense_sb[:], dense.rearrange("(p t) d -> p t d", t=TILES)).then_inc(s_dense, 16)
            for j in range(2, N_ONEHOT // 2):
                load_table(j)
            sp.dma_start(w1z_sb[0:ZP, :, :], w1z).then_inc(s_w1, 16)
            sp.dma_start(w1z_sb[ZP:ZP + 1, 0, :], b1).then_inc(s_w1, 16)
            sp.dma_start(w1d_sb[:], w1d).then_inc(s_w1, 16)
            sp.dma_start(w2_sb[:], w2.rearrange("(k p) n -> p k n", p=P)).then_inc(s_w2, 16)
            sp.dma_start(b2_sb[:], b2).then_inc(s_w2, 16)
            sp.dma_start(w3_sb[:], w3).then_inc(s_w2, 16)
            for j in range(N_ONEHOT // 2, N_ONEHOT):
                load_table(j)
            sp.wait_ge(s_ones, 1)
            for t in range(TILES):
                sp.wait_ge(s_z, HALVES * (t + 1))
                sp.dma_start(z_dram[t], z[:, t % 2]).then_inc(s_store[t % 2], 16)
                sp.wait_ge(s_store[t % 2], 16 * (t // 2 + 1))
                if t >= 2:
                    sp.wait_ge(s_h1m, 2 * (t - 1))
                sp.dma_start(zt[0:ZP, t % 2].rearrange("p q c g -> p q (c g)"), pair_rows(t)
                             ).then_inc(s_zt[t % 2], 16)
            sp.wait_ge(s_y, TILES)
            sp.dma_start(out.rearrange("(p t) o -> p (t o)", t=TILES), y_sb[:]).then_inc(s_out, 16)
            sp.wait_ge(s_out, 16)

        @block.gpsimd
        def _(pool):
            pool.wait_ge(s_ids, 16)
            for t in range(TILES):
                for n, f in enumerate(GATHERED):
                    nc.gpsimd.indirect_dma_start(
                        emb[:, t, n, :], None, tables[f],
                        bass.IndirectOffsetOnAxis(ap=ids_sb[:, t, f:f + 1], axis=0),
                    ).then_inc(s_gather[t][n // GRP], 16)

        @block.tensor
        def _(pe):
            n = 0

            def claim():
                if bank_free(n):
                    pe.wait_ge(*bank_free(n))

            pe.wait_ge(s_warm, 1)
            for _ in range(WARM):
                nc.tensor.matmul(h2_ps[0][:, :], warm[:, 0:P], warm[:, :], start=True, stop=True)
            pe.wait_ge(s_const, 16)
            for s in steps:
                if s[0] == "dense":
                    claim()
                    pe.wait_ge(s_dense, 16)
                    for t in range(TILES):
                        last = nc.tensor.transpose(bank_of(n)[:, t * P:(t + 1) * P], dense_sb[:, t, :], ident)
                    last.then_inc(s_full, 1)
                    n += 1
                elif s[0] == "onehot":
                    j, k = s[1], ktiles(s[1])
                    claim()
                    for half in range(2):
                        rows = range(half * (k // 2), (half + 1) * (k // 2))
                        pe.wait_ge(s_oh, 2 * j + half + 1)
                        for some in (rows[:-1], rows[-1:]):
                            if some == rows[-1:]:
                                pe.wait_ge(s_oha, j + 1)
                            for part in (table_hi, table_lo):
                                pe.wait_ge(*(high_part(j) if part is table_hi else (s_lo, j + 1)))
                                for row in some:
                                    last = nc.tensor.matmul(
                                        bank_of(n)[:, :], part[:, j % 2, row, :],
                                        onehot[:, (2 * j + half) % OHB, row - rows[0], :],
                                        start=(row == 0 and part is table_hi),
                                        stop=(row == k - 1 and part is table_lo))
                        if half == 0:
                            last.then_inc(s_ohused, 1)
                    last.then_inc(s_ohused, 1)
                    n += 1
                elif s[0] == "group":
                    _, t, g = s
                    claim()
                    pe.wait_ge(s_gather[t][g], 16 * len(GROUPS[g]))
                    for i in range(len(GROUPS[g])):
                        last = nc.tensor.transpose(bank_of(n)[:, i * P:(i + 1) * P],
                                                   emb[:, t, GRP * g + i, :], ident)
                    last.then_inc(s_full, 1)
                    n += 1
                elif s[0] == "gram":
                    _, t, half = s
                    if half == 0:
                        at = max(moves.index(("onehot", N_ONEHOT - 1)),
                                 moves.index(("group", t, len(GROUPS) - 1)))
                        for engine in (True, False):
                            pe.wait_ge(*empties(max(m for m in range(at + 1) if (m in by_dve) == engine)))
                    if t == 0:
                        pe.wait_ge(s_clear, 1)
                    else:
                        pe.wait_ge(s_z, HALVES * (t - 1) + half + 1)
                    for g in range(GH):
                        for q in range(QUADS):
                            x = cols[:, t, QG * q + GH * half + g, :]
                            last = nc.tensor.matmul(
                                gram[half][32 * q:32 * q + NF, NF * g:NF * (g + 1)], x, x,
                                start=True, stop=True, tile_position=(0, 32 * q))
                    last.then_inc(s_gram, 1)
                elif s[0] == "mlp1":
                    t = s[1]
                    if t == 0:
                        pe.wait_ge(s_w1, 48)
                        pe.wait_ge(s_w2, 48)
                    if t:
                        pe.wait_ge(s_h1, t)
                        pe.wait_ge(s_h1d, t)
                    for m in range(N1):
                        o = h1_ps[m // 2][:, (m % 2) * P:(m % 2 + 1) * P]
                        nc.tensor.matmul(o, w1d_sb[:, m * P:(m + 1) * P], dense_t[:, t, :],
                                         start=(m % 2 == 0), stop=False, skip_group_check=True)
                    pe.wait_ge(s_zt[t % 2], 16 * (t // 2 + 1))
                    for m in range(N1):
                        o = h1_ps[m // 2][:, (m % 2) * P:(m % 2 + 1) * P]
                        for c in range(ZC):
                            k = ZP + 1 if c == 0 else ZP
                            last = nc.tensor.matmul(o, w1z_sb[0:k, c, m * P:(m + 1) * P],
                                                    zt[0:k, t % 2, :, c, :], start=False,
                                                    stop=(c == ZC - 1), skip_group_check=True)
                        if m % 2:
                            last.then_inc(s_h1m, 1)
                elif s[0] == "mlp2":
                    t = s[1]
                    if t:
                        pe.wait_ge(s_h2, t)
                        pe.wait_ge(s_h2d, t)
                        pe.wait_ge(s_y, t)
                    for c in range(N1):
                        if c == 0:
                            pe.wait_ge(s_h1, t + 1)
                        if c == N1 // 2:
                            pe.wait_ge(s_h1d, t + 1)
                        for m in range(N2):
                            last = nc.tensor.matmul(h2_ps[m][:, 0:P], w2_sb[:, c, m * P:(m + 1) * P],
                                                    h1[:, c, :], start=(c == 0), stop=(c == N1 - 1))
                            if c == N1 - 1:
                                last.then_inc(s_h2m, 1)
                else:
                    t = s[1]
                    for m in range(N2):
                        pe.wait_ge(*((s_h2, t + 1) if m == 0 else (s_h2d, t + 1)))
                        last = nc.tensor.matmul(h2_ps[0][:, P:P + 1], h2[:, m, :], w3_sb[:, m:m + 1],
                                                start=(m == 0), stop=(m == N2 - 1))
                    last.then_inc(s_ym, 1)

        @block.scalar
        def _(act):
            act.dma_start(const_sb[:], consts).then_inc(s_const, 16)
            act.wait_ge(s_warm, 1)
            nc.scalar.activation(unread[:], warm[0:1, 0:1], ACT.Copy)

            def share(j):
                k = ktiles(j)
                act.wait_ge(s_idrow[j % TB], 16 * (j // TB + 1))
                if j:
                    act.wait_ge(s_oha, j)
                for half in range(2):
                    row = (half + 1) * (k // 2) - 1
                    nc.scalar.activation(distance[:, half, :], ids_row[0:TR, j % TB, :], ACT.Abs,
                                         bias=const_sb[0:TR, row_at(k, row, C_NEG)]).then_inc(s_dist, 1)
                if 2 * j >= OHB:
                    act.wait_ge(s_ohused, 2 * (j + 1) - OHB)
                act.wait_ge(s_dist, 2 * (j + 1))
                h = 2 * j % OHB
                nc.scalar.activation(onehot[:, h:h + 2, k // 2 - 1, :], distance[:], ACT.Relu,
                                     bias=1.0, scale=-1.0).then_inc(s_oha, 1)

            def part_hi(j):
                act.wait_ge(s_table[j % TB], 32 * (j // TB + 1))
                if j >= 2:
                    act.wait_ge(s_ohused, 2 * (j - 1))
                nc.scalar.activation(table_hi[:, j % 2, 0:ktiles(j), :], table[:, j % TB, 0:ktiles(j), :],
                                     ACT.Copy).then_inc(s_hi, 1)

            act.wait_ge(s_const, 16)
            share(0)
            n = 0
            for s in steps:
                if s in moves:
                    if s[0] == "dense":
                        act.wait_ge(*filled(n))
                        nc.scalar.activation(dense_t[:], column_in(n), ACT.Copy)
                    if s[0] == "onehot" and s[1] + 1 < N_ONEHOT:
                        part_hi(s[1] + 1)
                        share(s[1] + 1)
                    if n not in by_dve:
                        act.wait_ge(*filled(n))
                        nc.scalar.activation(column_out(n), column_in(n), ACT.Copy).then_inc(s_act, 1)
                    n += 1
                elif s[0] == "mlp1":
                    t = s[1]
                    act.wait_ge(s_h1m, 2 * t + 1)
                    if t:
                        act.wait_ge(s_h2m, N2 * t)
                    nc.scalar.activation(h1[:, 0:2, :], h1_ps[0][:, 0:2 * P].rearrange("p (m b) -> p m b", b=P),
                                         ACT.Relu).then_inc(s_h1, 1)
                elif s[0] == "mlp2":
                    t = s[1]
                    act.wait_ge(s_h2m, N2 * t + 1)
                    if t:
                        act.wait_ge(s_ym, t)
                    nc.scalar.activation(h2[:, 0, :], h2_ps[0][:, 0:P], ACT.Relu,
                                         bias=b2_sb[:, 0:1]).then_inc(s_h2, 1)

        @block.vector
        def _(dve):
            nc.vector.memset(warm[:], 1.0).then_inc(s_warm, 1)
            for half in range(HALVES):
                last = nc.vector.memset(gram[half][:, :], 0.0)
            last.then_inc(s_clear, 1)
            nc.vector.memset(zt[96:P], 1.0).then_inc(s_ones, 1)
            dve.wait_ge(s_const, 16)

            def prepare(j):
                k = ktiles(j)
                dve.wait_ge(s_idrow[j % TB], 16 * (j // TB + 1))
                for half in range(2):
                    h = 2 * j + half
                    if h >= OHB:
                        dve.wait_ge(s_ohused, h - OHB + 1)
                    for c in range(k // 2 - 1):
                        row = half * (k // 2) + c
                        last = nc.vector.tensor_scalar(
                            onehot[:, h % OHB, c, :], ids_row[0:TR, j % TB, :],
                            const_sb[0:TR, row_at(k, row, C_ROW)], None, ALU.is_equal)
                    last.then_inc(s_oh, 1)
                    if half == 0:
                        if j == 0:
                            dve.wait_ge(s_table[0], 32)
                            nc.vector.tensor_copy(table_hi[:, 0, 0:k, :], table[:, 0, 0:k, :]
                                                  ).then_inc(s_hi0, 1)
                        dve.wait_ge(s_table[j % TB], 32 * (j // TB + 1))
                        dve.wait_ge(*high_part(j))
                        if j >= 2:
                            dve.wait_ge(s_ohused, 2 * (j - 1))
                        nc.vector.tensor_tensor(table_lo[:, j % 2, 0:k, :], table[:, j % TB, 0:k, :],
                                                table_hi[:, j % 2, 0:k, :].bitcast(f32),
                                                ALU.subtract).then_inc(s_lo, 1)

            prepare(0)
            n = 0
            for s in steps:
                if s[0] == "onehot" and s[1] + 1 < N_ONEHOT:
                    prepare(s[1] + 1)
                if s in moves:
                    if n in by_dve:
                        dve.wait_ge(*filled(n))
                        nc.vector.tensor_copy(column_out(n), column_in(n)).then_inc(s_dve, 1)
                    n += 1
                elif s[0] == "gram":
                    _, t, half = s
                    if t >= 2:
                        dve.wait_ge(s_store[t % 2], 16 * (t // 2))
                    dve.wait_ge(s_gram, HALVES * t + half + 1)
                    g = gram[half][:, 0:GH * NF].rearrange("p (g j) -> p j g", j=NF)
                    o = z[:, t % 2, :, GH * half:GH * (half + 1)]
                    far, last = (const_sb[:, c:c + SLOTS].bitcast(i32).unsqueeze(2).to_broadcast([P, SLOTS, GH])
                                 for c in (C_FAR, C_LAST))
                    nc.vector.tensor_copy(o, g[:, 0:SLOTS, :]).then_inc(s_near, 1)
                    dve.wait_ge(s_near, HALVES * t + half + 1)
                    nc.vector.copy_predicated(o, far, g[:, SLOTS:2 * SLOTS, :]).then_inc(s_far, 1)
                    dve.wait_ge(s_far, HALVES * t + half + 1)
                    nc.vector.copy_predicated(o, last, g[:, NF - 1:NF, :].to_broadcast([P, SLOTS, GH])
                                              ).then_inc(s_z, 1)
                elif s[0] == "mlp1":
                    t = s[1]
                    dve.wait_ge(s_h1m, 2 * t + 2)
                    if t:
                        dve.wait_ge(s_h2m, N2 * t)
                    nc.vector.tensor_scalar(h1[:, 2:4, :], h1_ps[1][:, 0:2 * P].rearrange("p (m b) -> p m b", b=P),
                                            0.0, None, ALU.max).then_inc(s_h1d, 1)
                elif s[0] == "mlp2":
                    t = s[1]
                    dve.wait_ge(s_h2m, N2 * t + 2)
                    if t:
                        dve.wait_ge(s_ym, t)
                    nc.vector.tensor_scalar(h2[:, 1, :], h2_ps[1][:, 0:P], b2_sb[:, 1:2], 0.0,
                                            ALU.add, ALU.max).then_inc(s_h2d, 1)
                elif s[0] == "mlp3":
                    t = s[1]
                    dve.wait_ge(s_ym, t + 1)
                    nc.vector.tensor_copy(y_sb[:, t:t + 1], h2_ps[0][:, P:P + 1]).then_inc(s_y, 1)


def kernel(**inputs):
    import numpy as np
    import concourse.bacc as bacc
    from concourse.bass_utils import run_bass_kernel_spmd

    nc = bacc.Bacc("TRN2", target_bir_lowering=False, num_devices=1)
    arrays = {}

    def given(name, a):
        arrays[name] = a = np.ascontiguousarray(a)
        return nc.dram_tensor(name, a.shape, mybir.dt.from_np(a.dtype), kind="ExternalInput").ap()

    ids = np.asarray(inputs["ids"]).reshape(P, TILES, len(ROWS))
    w1 = np.asarray(inputs["W_top1"])
    iu, ju = np.triu_indices(NF, k=1)
    row_of = {(int(a), int(b)): r for r, (a, b) in enumerate(zip(iu, ju))}
    pair_rows = []
    consts = np.zeros((P, C_END), np.float32)
    consts[:, C_ID:C_ID + P] = np.eye(P)
    rows = np.concatenate([np.arange(P * k).reshape(P, k) for k in (8, 10)], axis=1)
    consts[:, C_ROW:C_ROW + 18] = rows
    consts[:, C_NEG:C_NEG + 18] = -rows
    for i in range(NF):
        for k in range(SLOTS):
            j = partner(k, i)
            a, b = sorted((ORDER[i], ORDER[j]))
            pair_rows.append(row_of[a, b])
            at = {k: None, k + SLOTS: C_FAR, NF - 1: C_LAST}[j] if i != k else C_LAST
            if at is not None:
                consts[i::32, at + k] = 1.0
    args = [
        given("dense", inputs["r_dense_features"]),
        given("ids", ids),
        given("ids_rows", ids.transpose(2, 1, 0).reshape(len(ROWS), TILES * P)),
        [given(f"tbl_{f}", inputs[f"tbl_{f}"]) for f in range(len(ROWS))],
        given("consts", consts),
        given("w1z", w1[pair_rows].reshape(ZP, ZC, H1)),
        given("w1d", w1[NPAIR:]),
        given("b1", np.asarray(inputs["b_top1"]).reshape(1, H1)),
        given("w2", inputs["W_top2"]),
        given("b2", np.asarray(inputs["b_top2"]).reshape(N2, P).T),
        given("w3", np.asarray(inputs["W_top3"]).reshape(N2, P).T),
        nc.dram_tensor("z_dram", (TILES, P, SLOTS, QG), mybir.dt.float32, kind="Internal").ap(),
        nc.dram_tensor("y", (TILES * P, 1), mybir.dt.float32, kind="ExternalOutput").ap(),
    ]
    build(nc, *args)
    r = run_bass_kernel_spmd(nc, [arrays], core_ids=[0])
    return r.results[0]["y"]
```
